# Optimizing a Trainium2 kernel written in Bass

```python
import numpy as np
import jax
import jax.numpy as jnp

def _softmax(x, axis=-1):
    return jax.nn.softmax(x, axis=axis)

def _gelu(x):
    return jax.nn.gelu(x, approximate=True)

def _silu(x):
    return jax.nn.silu(x)

def _sigmoid(x):
    return jax.nn.sigmoid(x)

def _layernorm(x, axis=-1, eps=1e-05):
    m = jnp.mean(x, axis=axis, keepdims=True)
    v = jnp.var(x, axis=axis, keepdims=True)
    return (x - m) / jnp.sqrt(v + eps)

def _scatter_add(tgt, idx, src, axis=0):
    return tgt.at[idx].add(src)

def _segment_sum(src, seg, n):
    return jax.ops.segment_sum(src, seg, n)
kernel_name = 'mk_cond_resid_d2_seqx_r4_ab7e6a'

def setup_inputs(seed: int=0):
    np.random.seed(seed)
    _w = jnp.asarray

    def _rec_inputs():
        import jax
        import jax.numpy as jnp
        _rk = jax.random.key(seed)
        x = -0.000125 + 0.9999 * jax.random.normal(jax.random.fold_in(_rk, 1), (8, 256, 256), jnp.float32)
        _lenS = 256 - jax.random.randint(jax.random.fold_in(_rk, 7), (8,), 0, max(1, 256 // 4) + 1, jnp.int32)
        _lenS2 = 256 - jax.random.randint(jax.random.fold_in(_rk, 8), (8,), 0, max(1, 256 // 4) + 1, jnp.int32)
        cond_1024 = -0.00493535 + 1.00056 * jax.random.normal(jax.random.fold_in(_rk, 11), (8, 256), jnp.float32)
        return (x, cond_1024)
    x, cond_1024 = _rec_inputs()

    def _L0_cond_setup():
        import jax, jax.numpy as jnp
        import numpy as np
        N, T, D, H = (64, 128, 256, 256)
        key = jax.random.key(seed)
        k1, k2, k3, k4 = jax.random.split(key, 4)
        x = jax.random.normal(k1, (N, T, D), dtype=jnp.float32)
        h0 = jax.random.normal(k2, (N, H), dtype=jnp.float32)
        Wx = jax.random.normal(k3, (D, H), dtype=jnp.float32) / np.sqrt(D)
        Wh = jax.random.normal(k4, (H, H), dtype=jnp.float32) / np.sqrt(H)
        b = jnp.zeros((H,), dtype=jnp.float32)
        return {'x': x, 'h0': h0, 'Wx': Wx, 'Wh': Wh, 'b': b}
    _L0_cond_all = _L0_cond_setup()
    _L0_cond_in = {k: v for k, v in _L0_cond_all.items() if k in ('Wx', 'Wh', 'b')}
    del _L0_cond_all

    def _L1_cond_setup():
        import jax, jax.numpy as jnp
        import numpy as np
        import math
        D = 256
        H = 256
        key = jax.random.key(seed)
        k1, k2, k3, k4 = jax.random.split(key, 4)
        x = jax.random.normal(k1, (64, 128, D), dtype=jnp.float32)
        h0 = jax.random.normal(k2, (64, H), dtype=jnp.float32)
        Wx = jax.random.normal(k3, (D, 4 * H), dtype=jnp.float32) / math.sqrt(D)
        Wh = jax.random.normal(k4, (H, 4 * H), dtype=jnp.float32) / math.sqrt(H)
        b = jnp.zeros((4 * H,), dtype=jnp.float32)
        return {'x': x, 'h0': h0, 'Wx': Wx, 'Wh': Wh, 'b': b}
    _L1_cond_all = _L1_cond_setup()
    _L1_cond_in = {k: v for k, v in _L1_cond_all.items() if k in ('Wx', 'Wh', 'b')}
    del _L1_cond_all
    return {'x': x, 'cond_1024': cond_1024, 'L0_cond_Wx': _L0_cond_in['Wx'], 'L0_cond_Wh': _L0_cond_in['Wh'], 'L0_cond_b': _L0_cond_in['b'], 'L1_cond_Wx': _L1_cond_in['Wx'], 'L1_cond_Wh': _L1_cond_in['Wh'], 'L1_cond_b': _L1_cond_in['b']}

def reference(x, cond_1024, L0_cond_Wx, L0_cond_Wh, L0_cond_b, L1_cond_Wx, L1_cond_Wh, L1_cond_b):
    import jax
    import jax.numpy as jnp

    def _L0_cond_ref(x, h0, Wx, Wh, b):
        import jax, jax.numpy as jnp
        import numpy as np
        N, T, D, H = (64, 128, 256, 256)
        xW = jnp.einsum('ntd,dh->nth', x, Wx) + b
        xW_t = jnp.swapaxes(xW, 0, 1)

        def step(prev_h, xw):
            next_h = jnp.tanh(prev_h @ Wh + xw)
            return (next_h, next_h)
        _, h_t = jax.lax.scan(step, h0, xW_t)
        return jnp.swapaxes(h_t, 0, 1)

    def _L1_cond_ref(x, h0, Wx, Wh, b):
        import jax, jax.numpy as jnp
        import numpy as np
        import math
        D = 256
        H = 256
        xz = jnp.einsum('ntd,dk->ntk', x, Wx) + b
        c0 = jnp.zeros_like(h0)

        def step(carry, xz_t):
            prev_h, prev_c = carry
            z = xz_t + prev_h @ Wh
            ai, af, ao, ag = jnp.split(z, 4, axis=1)
            i = jax.nn.sigmoid(ai)
            f = jax.nn.sigmoid(af)
            o = jax.nn.sigmoid(ao)
            g = jnp.tanh(ag)
            next_c = f * prev_c + i * g
            next_h = o * jnp.tanh(next_c)
            return ((next_h, next_c), next_h)
        _, hs = jax.lax.scan(step, (h0, c0), jnp.swapaxes(xz, 0, 1))
        return jnp.swapaxes(hs, 0, 1)
    x = x + _L0_cond_ref(x, cond_1024, L0_cond_Wx, L0_cond_Wh, L0_cond_b)
    x = x + _L1_cond_ref(x, cond_1024, L1_cond_Wx, L1_cond_Wh, L1_cond_b)
    return x

_drawn_inputs = setup_inputs


def setup_inputs(seed=0):
    import zlib

    import numpy as np

    out = dict(_drawn_inputs(seed))
    spreads = {'L0_cond_b': (0.0, 0.1), 'L1_cond_b': (0.0, 0.285)}
    factors = {}
    for name, (base, spread) in spreads.items():
        noise = np.random.default_rng([zlib.crc32(name.encode()), seed]).standard_normal(out[name].shape)
        drawn = base * np.exp(spread * noise) if base else spread * noise
        out[name] = jnp.asarray(drawn.astype(out[name].dtype))
    for name, factor in factors.items():
        out[name] = (out[name] * factor).astype(out[name].dtype)
    return out
```

```python
import concourse.bass as bass
from concourse import mybir
from contextlib import ExitStack

BATCH, T, D = 8, 256, 256
GATES = 4
TILES, LANES = 4, 32
HALVES = D // (TILES * LANES)
F = HALVES * LANES
PHASES = LANES // BATCH
GROUPS = T // PHASES
MAIN = 3 * F
SPARE = 32
WIDE = SPARE + F
SPLITS = 3
RING = 2
STEPS = RING * PHASES
LEAD = 2
LOOP_GROUPS = GROUPS - 2 * RING


def two_layer_program(nc, x, cond, rnn_wx_d, rnn_wh_d, rnn_b_d, lstm_wx_d, lstm_wh_d, lstm_b_d, out):
    fp32, bf16 = mybir.dt.float32, mybir.dt.bfloat16
    ALU = mybir.AluOpType
    TANH = mybir.ActivationFunctionType.Tanh
    COPY = mybir.ActivationFunctionType.Copy

    ctx = ExitStack()
    with ctx:
        def sbuf(name, shape, dtype=fp32):
            return ctx.enter_context(nc.sbuf_tensor(name, shape, dtype))

        def psum(name):
            return ctx.enter_context(nc.psum_tensor(name, [128, 512], fp32))

        def sem(name):
            return ctx.enter_context(nc.semaphore(name))

        rnn_wx = sbuf("rnn_wx", [128, HALVES, SPARE + TILES * F])
        rnn_wh = sbuf("rnn_wh", [128, HALVES, SPARE + TILES * F])
        lstm_wx = sbuf("lstm_wx", [128, HALVES, TILES, GATES * F])
        lstm_wh = sbuf("lstm_wh", [128, HALVES, TILES, GATES * F])
        rnn_b = sbuf("rnn_b", [LANES * SPLITS, SPARE + TILES * F])
        lstm_b = sbuf("lstm_b", [LANES * SPLITS, TILES * GATES * F])
        part = sbuf("part", [LANES * SPLITS, TILES * GATES * F], bf16)
        rnn_b_parts = sbuf("rnn_b_parts", [128, SPARE + TILES * F], bf16)
        lstm_b_parts = sbuf("lstm_b_parts", [128, TILES, GATES * F], bf16)
        ones = sbuf("ones", [128, LANES], bf16)
        x_down = sbuf("x_down", [128, GROUPS, HALVES, LANES])
        cond_down = sbuf("cond_down", [128, HALVES, BATCH])
        x_in = sbuf("x_in", [128, RING, HALVES, LANES])
        x1_in = sbuf("x1_in", [128, RING, HALVES, LANES])
        rnn_h = sbuf("rnn_h", [128, STEPS, HALVES, LANES])
        lstm_h = sbuf("lstm_h", [128, PHASES, HALVES, LANES])
        rnn_z = sbuf("rnn_z", [128, HALVES, LANES])
        lstm_z = sbuf("lstm_z", [128, 3 * HALVES, LANES])
        o_z = sbuf("o_z", [128, HALVES, LANES])
        gates = sbuf("gates", [128, 4 * HALVES, BATCH])
        tanh_o = sbuf("tanh_o", [128, HALVES, BATCH])
        terms = sbuf("terms", [128, 2 * HALVES, BATCH])
        tanh_c = sbuf("tanh_c", [128, HALVES, BATCH])
        y_down = sbuf("y_down", [128, RING, HALVES, LANES])

        rnn_acc = [psum(f"rnn_acc{r}") for r in range(RING)]
        lstm_acc = [psum(f"lstm_acc{r}") for r in range(RING)]
        o_acc = [psum(f"o_acc{r}") for r in range(RING)]

        x_loaded = sem("x_loaded")
        x_rest_loaded = sem("x_rest_loaded")
        cond_loaded = sem("cond_loaded")
        rnn_wx_loaded = sem("rnn_wx_loaded")
        rnn_wh_loaded = sem("rnn_wh_loaded")
        lstm_wx_loaded = sem("lstm_wx_loaded")
        lstm_wh_loaded = sem("lstm_wh_loaded")
        rnn_b_loaded = sem("rnn_b_loaded")
        lstm_b_loaded = sem("lstm_b_loaded")
        slot_free = [sem(f"slot_free{r}") for r in range(RING)]
        rnn_w_zeroed = sem("rnn_w_zeroed")
        b_zeroed = sem("b_zeroed")
        parts_zeroed = sem("parts_zeroed")
        b_step = sem("b_step")
        rnn_b_ready = sem("rnn_b_ready")
        lstm_b_ready = sem("lstm_b_ready")
        ones_ready = sem("ones_ready")
        rnn_h_zeroed = sem("rnn_h_zeroed")
        lstm_h_zeroed = sem("lstm_h_zeroed")
        lstm_wx_scaled = sem("lstm_wx_scaled")
        lstm_wh_scaled = sem("lstm_wh_scaled")
        rnn_z_ready = sem("rnn_z_ready")
        rnn_z_turned = sem("rnn_z_turned")
        rnn_h_ready = sem("rnn_h_ready")
        x1_ready = sem("x1_ready")
        lstm_z_ready = sem("lstm_z_ready")
        lstm_z_turned = sem("lstm_z_turned")
        o_z_ready = sem("o_z_ready")
        o_z_turned = sem("o_z_turned")
        gates_ready = sem("gates_ready")
        terms_ready = sem("terms_ready")
        c_ready = sem("c_ready")
        tanh_c_ready = sem("tanh_c_ready")
        lstm_h_ready = sem("lstm_h_ready")
        y_ready = sem("y_ready")
        x_in_ready = sem("x_in_ready")

        FIRST_X = LEAD + 1

        def cols(p):
            return slice(BATCH * (p % PHASES), BATCH * (p % PHASES + 1))

        block = ctx.enter_context(nc.Block())

        @block.sync
        def _(sp):
            sp.dma_start(x_down[:, 0:FIRST_X], x[:, 0:FIRST_X]).then_inc(x_loaded, 16)
            sp.dma_start(rnn_wx[:, :, SPARE:], rnn_wx_d).then_inc(rnn_wx_loaded, 16)
            sp.dma_start(rnn_wh[:, :, SPARE:], rnn_wh_d).then_inc(rnn_wh_loaded, 16)
            sp.dma_start(lstm_wh[:], lstm_wh_d).then_inc(lstm_wh_loaded, 16)
            sp.dma_start(x_down[:, FIRST_X:GROUPS], x[:, FIRST_X:GROUPS]).then_inc(x_rest_loaded, 16)

            def store(g, r):
                sp.wait_ge(y_ready, g * PHASES + PHASES)
                sp.dma_start(out[:, bass.ds(g, 1)], y_down[:, r:r + 1]).then_inc(slot_free[r], 16)

            with sp.Fori(0, GROUPS // RING) as n:
                for r in range(RING):
                    store(n * RING + r, r)
            for r in range(RING):
                sp.wait_ge(slot_free[r], 16 + 16 * GROUPS // RING)

        @block.gpsimd
        def _(pool):
            nc.gpsimd.memset(rnn_b_parts[:], 0.0).then_inc(parts_zeroed, 1)
            nc.gpsimd.memset(lstm_b_parts[:], 0.0).then_inc(parts_zeroed, 1)

            def add_x1(x_group, r, p):
                nc.gpsimd.tensor_tensor(x1_in[:, r, :, cols(p)], x_group[:, :, cols(p)],
                                        rnn_h[:, (PHASES * r + p + 1) % STEPS, :, cols(p + 1)],
                                        ALU.add).then_inc(x1_ready, 1)

            def copy_x(g, r):
                nc.gpsimd.tensor_copy(x_in[:, r], x_down[:, bass.ds(g, 1)].rearrange("q o k c -> q (o k) c")) \
                    .then_inc(x_in_ready, 1)

            def period(g, r, rnn=True, next_x=True):
                for p in range(PHASES):
                    if rnn:
                        if p == 0:
                            pool.wait_ge(x_in_ready, g + 1)
                            pool.wait_ge(x1_ready, (g + LEAD) * PHASES)
                        pool.wait_ge(rnn_h_ready, (g + LEAD) * PHASES + p + 2)
                        pool.wait_ge(y_ready, g * PHASES + p + 1)
                        add_x1(x_in[:, r], r, p)
                    if next_x and p == 0:
                        copy_x(g + LEAD + 1, (r + LEAD + 1) % RING)

            pool.wait_ge(x_loaded, 16)
            for g in range(LEAD):
                for p in range(PHASES):
                    pool.wait_ge(rnn_h_ready, g * PHASES + p + 2)
                    add_x1(x_down[:, g], g, p)
            copy_x(LEAD, 0)
            pool.wait_ge(x_rest_loaded, 16)
            with pool.Fori(0, LOOP_GROUPS // RING) as n:
                for r in range(RING):
                    period(n * RING + r, r)
            for g in range(LOOP_GROUPS, GROUPS - LEAD):
                period(g, g % RING, next_x=g + LEAD + 1 < GROUPS)

        @block.scalar
        def _(act):
            act.dma_start(cond_down[:], cond).then_inc(cond_loaded, 16)
            act.wait_ge(b_zeroed, 1)
            for n in range(SPLITS):
                act.dma_start(rnn_b[LANES * n:LANES * n + 1, SPARE:], rnn_b_d).then_inc(rnn_b_loaded, 16)
            act.dma_start(lstm_wx[:], lstm_wx_d).then_inc(lstm_wx_loaded, 16)
            act.wait_ge(b_zeroed, 2)
            for n in range(SPLITS):
                act.dma_start(lstm_b[LANES * n:LANES * n + 1], lstm_b_d).then_inc(lstm_b_loaded, 16)
            act.wait_ge(cond_loaded, 16)
            act.wait_ge(rnn_h_zeroed, 1)
            nc.scalar.activation(rnn_h[:, 0, :, cols(0)], cond_down[:], COPY).then_inc(rnn_h_ready, 1)

            def rnn_tanh(s, r, p):
                slot = (PHASES * r + p + 1) % STEPS
                act.wait_ge(rnn_z_turned, s + 1)
                nc.scalar.activation(rnn_h[:, slot, :, cols(p + 1)], rnn_z[:, :, cols(p)], TANH) \
                    .then_inc(rnn_h_ready, 1)

            def period(g, r, rnn=True):
                for p in range(PHASES):
                    t = g * PHASES + p
                    act.wait_ge(lstm_z_turned, t + 1)
                    nc.scalar.activation(gates[:, 0:3 * HALVES], lstm_z[:, :, cols(p)], TANH).then_inc(gates_ready, 1)
                    act.wait_ge(o_z_turned, t + 1)
                    nc.scalar.activation(tanh_o[:], o_z[:, :, cols(p)], TANH)
                    act.wait_ge(c_ready, t + 2)
                    nc.scalar.activation(tanh_c[:], gates[:, 3 * HALVES:], TANH, scale=0.5).then_inc(tanh_c_ready, 1)
                    if rnn:
                        rnn_tanh((g + LEAD) * PHASES + p, r, p)

            for s in range(STEPS):
                rnn_tanh(s, s // PHASES, s % PHASES)
            with act.Fori(0, LOOP_GROUPS // RING) as n:
                for r in range(RING):
                    period(n * RING + r, r)
            for g in range(LOOP_GROUPS, GROUPS):
                period(g, g % RING, rnn=g + LEAD < GROUPS)

        @block.vector
        def _(dve):
            nc.vector.memset(rnn_b[:], 0.0).then_inc(b_zeroed, 1)
            nc.vector.memset(rnn_h[:], 0.0).then_inc(rnn_h_zeroed, 1)
            nc.vector.memset(lstm_b[:], 0.0).then_inc(b_zeroed, 1)
            nc.vector.memset(ones[:], 0.0).then_inc(ones_ready, 1)
            dve.wait_ge(ones_ready, 1)
            for n in range(SPLITS):
                nc.vector.memset(ones[LANES * n:LANES * n + 1], 1.0).then_inc(ones_ready, 1)
            nc.vector.memset(rnn_wx[:, :, 0:SPARE], 0.0).then_inc(rnn_w_zeroed, 1)
            nc.vector.memset(rnn_wh[:, :, 0:SPARE], 0.0).then_inc(rnn_w_zeroed, 1)
            nc.vector.memset(lstm_h[:], 0.0).then_inc(lstm_h_zeroed, 1)
            nc.vector.memset(gates[:, 3 * HALVES:], 0.0).then_inc(c_ready, 1)
            for r in range(RING):
                nc.vector.memset(y_down[:, r], 0.0).then_inc(slot_free[r], 16)
            dve.wait_ge(cond_loaded, 16)
            dve.wait_ge(lstm_h_zeroed, 1)
            nc.vector.tensor_scalar(lstm_h[:, 0, :, cols(0)], cond_down[:], 2.0, None, ALU.mult).then_inc(lstm_h_ready, 1)

            def rnn_turn(s, r):
                dve.wait_ge(rnn_z_ready, s + 1)
                nc.vector.transpose(rnn_z[:].rearrange("q k c -> q (k c)"), rnn_acc[r][:, SPARE:WIDE]).then_inc(rnn_z_turned, 1)

            def scale(w, sigmoid, tanh, signal):
                for columns, factor in ((slice(0, 2 * F), sigmoid), (slice(2 * F, MAIN), tanh),
                                        (slice(MAIN, GATES * F), sigmoid)):
                    if factor != 1.0:
                        nc.vector.tensor_scalar(w[:, :, columns], w[:, :, columns], factor, None, ALU.mult) \
                            .then_inc(signal, 1)

            def period(n, g, r, rnn=True):
                for p in range(PHASES):
                    t = g * PHASES + p
                    dve.wait_ge(lstm_z_ready, t + 1)
                    nc.vector.transpose(lstm_z[:].rearrange("q k c -> q (k c)"), lstm_acc[r][:, 0:MAIN]) \
                        .then_inc(lstm_z_turned, 1)
                    dve.wait_ge(o_z_ready, t + 1)
                    nc.vector.transpose(o_z[:].rearrange("q k c -> q (k c)"), o_acc[r][:, SPARE:WIDE]) \
                        .then_inc(o_z_turned, 1)
                    dve.wait_ge(gates_ready, t + 1)
                    nc.vector.scalar_tensor_tensor(out=terms[:], in0=gates[:, 0:2 * HALVES], scalar=1.0,
                                                   in1=gates[:, 2 * HALVES:4 * HALVES],
                                                   op0=ALU.add, op1=ALU.mult).then_inc(terms_ready, 1)
                    dve.wait_ge(terms_ready, t + 1)
                    nc.vector.scalar_tensor_tensor(out=gates[:, 3 * HALVES:], in0=terms[:, HALVES:], scalar=0.5,
                                                   in1=terms[:, 0:HALVES],
                                                   op0=ALU.mult, op1=ALU.add).then_inc(c_ready, 1)
                    dve.wait_ge(tanh_c_ready, t + 1)
                    h = lstm_h[:, (p + 1) % PHASES, :, cols(p + 1)]
                    nc.vector.scalar_tensor_tensor(out=h, in0=tanh_o[:], scalar=1.0,
                                                   in1=tanh_c[:], op0=ALU.add, op1=ALU.mult).then_inc(lstm_h_ready, 1)
                    if p == 0:
                        dve.wait_ge(slot_free[r], n * 16 + 16)
                    dve.wait_ge(x1_ready, t + 1)
                    dve.wait_ge(lstm_h_ready, t + 2)
                    nc.vector.scalar_tensor_tensor(out=y_down[:, r, :, cols(p)], in0=h, scalar=0.5,
                                                   in1=x1_in[:, r, :, cols(p)],
                                                   op0=ALU.mult, op1=ALU.add).then_inc(y_ready, 1)
                    if rnn:
                        rnn_turn((g + LEAD) * PHASES + p, r)

            chain = [0]

            def link(instruction):
                instruction.then_inc(b_step, 1)
                chain[0] += 1
                dve.wait_ge(b_step, chain[0])

            def split(n, b, parts, signal):
                row = slice(LANES * n, LANES * n + 1)
                if n + 1 < SPLITS:
                    link(nc.vector.tensor_copy(part[:, 0:b.shape[-1]], b))
                    nc.vector.tensor_copy(parts[row], part[row, 0:b.shape[-1]]).then_inc(signal, 1)
                    link(nc.vector.tensor_tensor(b, b, part[:, 0:b.shape[-1]], ALU.subtract))
                else:
                    nc.vector.tensor_copy(parts[row], b[row]).then_inc(signal, 1)

            dve.wait_ge(parts_zeroed, 2)
            dve.wait_ge(rnn_b_loaded, 16 * SPLITS)
            for n in range(SPLITS):
                split(n, rnn_b[:], rnn_b_parts, rnn_b_ready)
            b_gates = lstm_b[:].rearrange("q (j n) -> q j n", j=TILES)
            b_parts = lstm_b_parts[:].rearrange("q j n -> q (j n)")
            for s in range(STEPS):
                rnn_turn(s, s // PHASES)
                if s == 0:
                    dve.wait_ge(lstm_wx_loaded, 16)
                    for k in range(HALVES):
                        scale(lstm_wx[:, k], 0.5, 1.0, lstm_wx_scaled)
                if s == 1:
                    dve.wait_ge(lstm_b_loaded, 16 * SPLITS)
                    link(nc.vector.tensor_scalar(b_gates[:, :, 0:2 * F], b_gates[:, :, 0:2 * F], 0.5, None, ALU.mult))
                    link(nc.vector.tensor_scalar(b_gates[:, :, MAIN:], b_gates[:, :, MAIN:], 0.5, None, ALU.mult))
                if s == 2:
                    dve.wait_ge(lstm_wh_loaded, 16)
                    for k in range(HALVES):
                        scale(lstm_wh[:, k], 0.25, 0.5, lstm_wh_scaled)
                if 3 <= s < 3 + SPLITS:
                    split(s - 3, lstm_b[:], b_parts, lstm_b_ready)
            with dve.Fori(0, LOOP_GROUPS // RING) as n:
                for r in range(RING):
                    period(n, n * RING + r, r)
            for g in range(LOOP_GROUPS, GROUPS):
                period(g // RING, g, g % RING, rnn=g + LEAD < GROUPS)

        @block.tensor
        def _(pe):
            def add_product(acc, stationary, columns, start=False):
                m = stationary.shape[-1]
                for j in range(TILES):
                    moving = columns(j)
                    last = nc.tensor.matmul(acc[LANES * j:LANES * j + m, 0:moving.shape[-1]], stationary, moving,
                                            start=start, stop=True, skip_group_check=True,
                                            tile_position=(0, LANES * j))
                return last

            def rnn_columns(w):
                return lambda j: w[:, F * j:F * j + WIDE]

            def main_columns(w):
                return lambda j: w[:, j, 0:MAIN]

            def o_columns(w):
                return lambda j: w[:, j, MAIN - SPARE:MAIN + F]

            def rnn_input(r, stationary):
                for k in range(HALVES):
                    add_product(rnn_acc[r], stationary[:, k], rnn_columns(rnn_wx[:, k]), start=k == 0)

            def rnn_bias(r):
                add_product(rnn_acc[r], ones[:], rnn_columns(rnn_b_parts[:]))

            def lstm_input(r, k, acc, columns):
                add_product(acc[r], x1_in[:, r, k], columns(lstm_wx[:, k]), start=k == 0)

            def lstm_bias(r, acc, columns):
                add_product(acc[r], ones[:], columns(lstm_b_parts[:]))

            def rnn_step(s, r, p):
                slot, m = PHASES * r + p, BATCH * (p + 1)
                pe.wait_ge(rnn_h_ready, s + 1)
                for k in range(HALVES):
                    last = add_product(rnn_acc[r], rnn_h[:, slot, k, 0:m], rnn_columns(rnn_wh[:, k]))
                last.then_inc(rnn_z_ready, 1)

            def lstm_step(t, r, p):
                m = BATCH * (p + 1)
                pe.wait_ge(lstm_h_ready, t + 1)
                for acc, columns, signal in ((lstm_acc, main_columns, lstm_z_ready), (o_acc, o_columns, o_z_ready)):
                    for k in range(HALVES):
                        last = add_product(acc[r], lstm_h[:, p, k, 0:m], columns(lstm_wh[:, k]))
                    last.then_inc(signal, 1)

            def prepare_lstm(part, r):
                if part < HALVES:
                    lstm_input(r, part, lstm_acc, main_columns)
                elif part == HALVES:
                    for k in range(HALVES):
                        lstm_input(r, k, o_acc, o_columns)
                if part == 1:
                    lstm_bias(r, lstm_acc, main_columns)
                if part == 2:
                    lstm_bias(r, o_acc, o_columns)

            def period(g, r, rnn=True, next_rnn=True, next_lstm=True):
                nxt = (r + 1) % RING
                for p in range(PHASES):
                    lstm_step(g * PHASES + p, r, p)
                    if rnn:
                        rnn_step((g + LEAD) * PHASES + p, r, p)
                    if next_lstm:
                        if p == 0:
                            pe.wait_ge(x1_ready, (g + 2) * PHASES)
                        prepare_lstm(p, nxt)
                    if next_rnn and p == PHASES - 1:
                        pe.wait_ge(x_in_ready, g + 2)
                        rnn_input(nxt, x_in[:, nxt])
                        rnn_bias(nxt)

            pe.wait_ge(x_loaded, 16)
            pe.wait_ge(rnn_w_zeroed, 2)
            pe.wait_ge(rnn_wx_loaded, 16)
            rnn_input(0, x_down[:, 0])
            rnn_input(1, x_down[:, 1])
            pe.wait_ge(ones_ready, 1 + SPLITS)
            pe.wait_ge(rnn_b_ready, SPLITS)
            rnn_bias(0)
            rnn_bias(1)
            pe.wait_ge(rnn_wh_loaded, 16)
            for s in range(STEPS):
                rnn_step(s, s // PHASES, s % PHASES)
                if s == PHASES:
                    rnn_input(0, x_down[:, LEAD])
                    rnn_bias(0)
                    pe.wait_ge(lstm_wx_scaled, 2 * HALVES)
                    pe.wait_ge(x1_ready, PHASES)
                if s == PHASES + 1:
                    pe.wait_ge(lstm_b_ready, SPLITS)
                if s >= PHASES:
                    prepare_lstm(s - PHASES, 0)
            pe.wait_ge(lstm_wh_scaled, 3 * HALVES)
            with pe.Fori(0, LOOP_GROUPS // RING) as n:
                for r in range(RING):
                    period(n * RING + r, r)
            for g in range(LOOP_GROUPS, GROUPS):
                period(g, g % RING, rnn=g + LEAD < GROUPS, next_rnn=g + LEAD + 1 < GROUPS,
                       next_lstm=g + 1 < GROUPS)


def kernel(x, cond_1024, L0_cond_Wx, L0_cond_Wh, L0_cond_b, L1_cond_Wx, L1_cond_Wh, L1_cond_b):
    import numpy as np
    import concourse.bacc as bacc
    from concourse.bass_utils import run_bass_kernel_spmd

    def down(a):
        return a.reshape(TILES, HALVES, LANES, *a.shape[1:]).swapaxes(1, 2).reshape(TILES * LANES, HALVES, *a.shape[1:])

    def by_tile(w):
        w = w.reshape(*w.shape[:-1], -1, TILES, F)
        w = w[..., [0, 1, 3, 2], :, :] if w.shape[-3] == GATES else w
        w = np.moveaxis(w, -2, -3)
        return w.reshape(*w.shape[:-3], TILES, -1)

    def weights(w):
        return by_tile(down(np.asarray(w)))

    xt = np.asarray(x).reshape(BATCH, GROUPS, PHASES, D).transpose(3, 1, 2, 0).reshape(D, GROUPS, LANES)
    arrays = {
        "x": down(xt).transpose(0, 2, 1, 3),
        "cond": down(np.asarray(cond_1024).T),
        "rnn_wx": down(np.asarray(L0_cond_Wx)), "rnn_wh": down(np.asarray(L0_cond_Wh)),
        "rnn_b": np.asarray(L0_cond_b)[None],
        "lstm_wx": weights(L1_cond_Wx), "lstm_wh": weights(L1_cond_Wh),
        "lstm_b": by_tile(np.asarray(L1_cond_b)[None]).reshape(1, -1),
    }
    arrays = {f"{name}_dram": np.ascontiguousarray(a) for name, a in arrays.items()}
    nc = bacc.Bacc("TRN2", target_bir_lowering=False, num_devices=1)
    args = [nc.dram_tensor(name, a.shape, mybir.dt.from_np(a.dtype), kind="ExternalInput").ap()
            for name, a in arrays.items()]
    out = nc.dram_tensor("y_dram", (TILES * LANES, GROUPS, HALVES, LANES), mybir.dt.float32, kind="ExternalOutput").ap()
    two_layer_program(nc, *args, out)
    got = run_bass_kernel_spmd(nc, [arrays], core_ids=[0]).results[0]["y_dram"]
    got = got.reshape(TILES, LANES, GROUPS, HALVES, PHASES, BATCH).transpose(5, 2, 4, 0, 3, 1)
    return np.ascontiguousarray(got.reshape(BATCH, T, D))
```

```python
import concourse.bass as bass
from concourse import mybir
from contextlib import ExitStack

BATCH, T, D = 8, 256, 256
GATES = 4
TILES, LANES = 4, 32
HALVES = D // (TILES * LANES)
F = HALVES * LANES
PHASES = LANES // BATCH
GROUPS = T // PHASES
MAIN = 3 * F
SPARE = 32
WIDE = SPARE + F
SPLITS = 3
RING = 2
STEPS = RING * PHASES
LEAD = 6
LOOP_GROUPS = GROUPS - 2 * RING


def two_layer_program(nc, x, cond, rnn_wx_d, rnn_wh_d, rnn_b_d, lstm_wx_d, lstm_wh_d, lstm_b_d, out):
    fp32, bf16 = mybir.dt.float32, mybir.dt.bfloat16
    ALU = mybir.AluOpType
    TANH = mybir.ActivationFunctionType.Tanh
    COPY = mybir.ActivationFunctionType.Copy

    ctx = ExitStack()
    with ctx:
        def sbuf(name, shape, dtype=fp32):
            return ctx.enter_context(nc.sbuf_tensor(name, shape, dtype))

        def psum(name):
            return ctx.enter_context(nc.psum_tensor(name, [128, 512], fp32))

        def sem(name):
            return ctx.enter_context(nc.semaphore(name))

        rnn_wx = sbuf("rnn_wx", [128, HALVES, SPARE + TILES * F])
        rnn_wh = sbuf("rnn_wh", [128, HALVES, SPARE + TILES * F])
        lstm_wx = sbuf("lstm_wx", [128, HALVES, TILES, GATES * F])
        lstm_wh = sbuf("lstm_wh", [128, HALVES, TILES, GATES * F])
        rnn_b = sbuf("rnn_b", [128, HALVES])
        lstm_b = sbuf("lstm_b", [TILES, GATES * F])
        b_split = sbuf("b_split", [TILES, SPLITS, GATES * F], bf16)
        lstm_b_parts = sbuf("lstm_b_parts", [128, TILES, GATES * F], bf16)
        ones = sbuf("ones", [128, LANES], bf16)
        x_down = sbuf("x_down", [128, GROUPS, HALVES, LANES])
        cond_down = sbuf("cond_down", [128, HALVES, BATCH])
        x_in = sbuf("x_in", [128, RING, HALVES, LANES])
        x1_in = sbuf("x1_in", [128, RING, HALVES, LANES])
        rnn_h = sbuf("rnn_h", [128, STEPS, HALVES, LANES])
        lstm_h = sbuf("lstm_h", [128, PHASES, HALVES, LANES])
        rnn_z = sbuf("rnn_z", [128, HALVES, LANES])
        o_z = sbuf("o_z", [128, HALVES, LANES])
        gates = sbuf("gates", [128, 4 * HALVES, BATCH])
        tanh_o = sbuf("tanh_o", [128, HALVES, BATCH])
        terms = sbuf("terms", [128, 2 * HALVES, BATCH])
        y_down = sbuf("y_down", [128, RING, HALVES, LANES])

        rnn_acc = [psum(f"rnn_acc{r}") for r in range(RING)]
        lstm_acc = [psum(f"lstm_acc{r}") for r in range(RING)]
        o_acc = [psum(f"o_acc{r}") for r in range(RING)]
        lstm_z = psum("lstm_z")[:, 0:3 * HALVES * LANES].rearrange("q (k c) -> q k c", c=LANES)
        states = psum("states")[:, 0:2 * HALVES * BATCH].rearrange("q (k b) -> q k b", b=BATCH)
        new_c, tanh_c = states[:, 0:HALVES], states[:, HALVES:]

        x_loaded = sem("x_loaded")
        x_rest_loaded = sem("x_rest_loaded")
        cond_loaded = sem("cond_loaded")
        rnn_wx_loaded = sem("rnn_wx_loaded")
        rnn_wh_loaded = sem("rnn_wh_loaded")
        lstm_wx_loaded = sem("lstm_wx_loaded")
        lstm_wh_loaded = sem("lstm_wh_loaded")
        rnn_b_loaded = sem("rnn_b_loaded")
        lstm_b_loaded = sem("lstm_b_loaded")
        slot_free = [sem(f"slot_free{r}") for r in range(RING)]
        rnn_w_zeroed = sem("rnn_w_zeroed")
        parts_zeroed = sem("parts_zeroed")
        b_step = sem("b_step")
        lstm_b_ready = sem("lstm_b_ready")
        ones_ready = sem("ones_ready")
        rnn_h_zeroed = sem("rnn_h_zeroed")
        lstm_h_zeroed = sem("lstm_h_zeroed")
        lstm_wx_scaled = sem("lstm_wx_scaled")
        lstm_wh_scaled = sem("lstm_wh_scaled")
        rnn_z_ready = sem("rnn_z_ready")
        rnn_z_turned = sem("rnn_z_turned")
        rnn_h_ready = sem("rnn_h_ready")
        x1_ready = sem("x1_ready")
        lstm_z_ready = sem("lstm_z_ready")
        lstm_z_turned = sem("lstm_z_turned")
        o_z_ready = sem("o_z_ready")
        o_z_turned = sem("o_z_turned")
        gates_ready = sem("gates_ready")
        terms_ready = sem("terms_ready")
        c_ready = sem("c_ready")
        tanh_c_ready = sem("tanh_c_ready")
        lstm_h_ready = sem("lstm_h_ready")
        y_ready = sem("y_ready")
        x_in_ready = sem("x_in_ready")

        FIRST_X = 3

        def cols(p):
            return slice(BATCH * (p % PHASES), BATCH * (p % PHASES + 1))

        def place(s):
            return s // PHASES % RING, s % PHASES

        block = ctx.enter_context(nc.Block())

        @block.sync
        def _(sp):
            sp.dma_start(x_down[:, 0:FIRST_X], x[:, 0:FIRST_X]).then_inc(x_loaded, 16)
            sp.dma_start(rnn_wx[:, :, SPARE:], rnn_wx_d).then_inc(rnn_wx_loaded, 16)
            sp.dma_start(rnn_wh[:, :, SPARE:], rnn_wh_d).then_inc(rnn_wh_loaded, 16)
            sp.dma_start(lstm_wx[:], lstm_wx_d).then_inc(lstm_wx_loaded, 16)
            sp.dma_start(lstm_wh[:], lstm_wh_d).then_inc(lstm_wh_loaded, 16)
            sp.dma_start(x_down[:, FIRST_X:GROUPS], x[:, FIRST_X:GROUPS]).then_inc(x_rest_loaded, 16)

            def store(g, r):
                sp.wait_ge(y_ready, g * PHASES + PHASES)
                sp.dma_start(out[:, bass.ds(g, 1)], y_down[:, r:r + 1]).then_inc(slot_free[r], 16)

            with sp.Fori(0, GROUPS // RING) as n:
                for r in range(RING):
                    store(n * RING + r, r)
            for r in range(RING):
                sp.wait_ge(slot_free[r], 16 + 16 * GROUPS // RING)

        @block.gpsimd
        def _(pool):
            nc.gpsimd.memset(lstm_b_parts[:], 0.0).then_inc(parts_zeroed, 1)

            pool.wait_ge(parts_zeroed, 1)
            pool.wait_ge(b_step, 1 + 2 * SPLITS)
            for n in range(SPLITS):
                pool.dma_start(lstm_b_parts[LANES * n:LANES * n + 1], b_split[:, n]).then_inc(lstm_b_ready, 16)

            def add_x1(x_group, s):
                r, p = place(s)
                nc.gpsimd.tensor_tensor(x1_in[:, r, :, cols(p)], x_group[:, :, cols(p)],
                                        rnn_h[:, (s + 1) % STEPS, :, cols(p + 1)], ALU.add).then_inc(x1_ready, 1)

            def copy_x(g, r):
                nc.gpsimd.tensor_copy(x_in[:, r], x_down[:, bass.ds(g, 1)].rearrange("q o k c -> q (o k) c")) \
                    .then_inc(x_in_ready, 1)

            def period(g, r, steps=PHASES, next_x=True):
                for p in range(steps):
                    if p == 2:
                        pool.wait_ge(x_in_ready, g + 2)
                        pool.wait_ge(x1_ready, (g + 2) * PHASES)
                    pool.wait_ge(rnn_h_ready, g * PHASES + p + LEAD + 2)
                    add_x1(x_in[:, place(PHASES * r + p + LEAD)[0]], PHASES * r + p + LEAD)
                    if next_x and p == 2:
                        copy_x(g + 3, (r + 1) % RING)

            pool.wait_ge(x_loaded, 16)
            for s in range(LEAD):
                pool.wait_ge(rnn_h_ready, s + 2)
                add_x1(x_down[:, s // PHASES], s)
            copy_x(1, 1)
            copy_x(2, 0)
            pool.wait_ge(x_in_ready, 2)
            pool.wait_ge(x_rest_loaded, 16)
            with pool.Fori(0, LOOP_GROUPS // RING) as n:
                for r in range(RING):
                    period(n * RING + r, r)
            for g in range(LOOP_GROUPS, GROUPS - 1):
                period(g, g % RING, steps=min(PHASES, T - LEAD - g * PHASES), next_x=g + 3 < GROUPS)

        @block.scalar
        def _(act):
            act.dma_start(cond_down[:], cond).then_inc(cond_loaded, 16)
            act.dma_start(rnn_b[:], rnn_b_d).then_inc(rnn_b_loaded, 16)
            act.dma_start(lstm_b[:], lstm_b_d).then_inc(lstm_b_loaded, 16)
            act.wait_ge(cond_loaded, 16)
            act.wait_ge(rnn_h_zeroed, 1)
            nc.scalar.activation(rnn_h[:, 0, :, cols(0)], cond_down[:], COPY).then_inc(rnn_h_ready, 1)

            def rnn_tanh(done, s):
                p = s % PHASES
                act.wait_ge(rnn_z_turned, done)
                for k in range(HALVES):
                    last = nc.scalar.activation(rnn_h[:, (s + 1) % STEPS, k, cols(p + 1)], rnn_z[:, k, cols(p)], TANH,
                                                bias=rnn_b[:, k:k + 1])
                last.then_inc(rnn_h_ready, 1)

            def period(g, r, rnn_steps=PHASES):
                for p in range(PHASES):
                    t = g * PHASES + p
                    act.wait_ge(lstm_z_turned, t + 1)
                    nc.scalar.activation(gates[:, 0:3 * HALVES], lstm_z[:, :, cols(p)], TANH).then_inc(gates_ready, 1)
                    act.wait_ge(o_z_turned, t + 1)
                    nc.scalar.activation(tanh_o[:], o_z[:, :, cols(p)], TANH)
                    act.wait_ge(c_ready, t + 2)
                    nc.scalar.activation(tanh_c, new_c, TANH, scale=0.5).then_inc(tanh_c_ready, 1)
                    if p < rnn_steps:
                        rnn_tanh(t + LEAD + 1, PHASES * r + p + LEAD)

            act.wait_ge(rnn_b_loaded, 16)
            for s in range(LEAD):
                rnn_tanh(s + 1, s)
            with act.Fori(0, LOOP_GROUPS // RING) as n:
                for r in range(RING):
                    period(n * RING + r, r)
            for g in range(LOOP_GROUPS, GROUPS):
                period(g, g % RING, rnn_steps=T - LEAD - g * PHASES)

        @block.vector
        def _(dve):
            nc.vector.memset(rnn_h[:], 0.0).then_inc(rnn_h_zeroed, 1)
            nc.vector.memset(ones[:], 0.0).then_inc(ones_ready, 1)
            dve.wait_ge(ones_ready, 1)
            for n in range(SPLITS):
                nc.vector.memset(ones[LANES * n:LANES * n + 1], 1.0).then_inc(ones_ready, 1)
            nc.vector.memset(rnn_wx[:, :, 0:SPARE], 0.0).then_inc(rnn_w_zeroed, 1)
            nc.vector.memset(rnn_wh[:, :, 0:SPARE], 0.0).then_inc(rnn_w_zeroed, 1)
            nc.vector.memset(lstm_h[:], 0.0).then_inc(lstm_h_zeroed, 1)
            nc.vector.memset(gates[:, 3 * HALVES:], 0.0).then_inc(c_ready, 1)
            for r in range(RING):
                nc.vector.memset(y_down[:, r], 0.0).then_inc(slot_free[r], 16)
            dve.wait_ge(cond_loaded, 16)
            dve.wait_ge(lstm_h_zeroed, 1)
            nc.vector.tensor_scalar(lstm_h[:, 0, :, cols(0)], cond_down[:], 2.0, None, ALU.mult).then_inc(lstm_h_ready, 1)

            def rnn_turn(done, s):
                dve.wait_ge(rnn_z_ready, done)
                nc.vector.transpose(rnn_z[:].rearrange("q k c -> q (k c)"), rnn_acc[place(s)[0]][:, SPARE:WIDE]) \
                    .then_inc(rnn_z_turned, 1)

            def scale(w, sigmoid, tanh, signal):
                for columns, factor in ((slice(0, 2 * F), sigmoid), (slice(2 * F, MAIN), tanh),
                                        (slice(MAIN, GATES * F), sigmoid)):
                    if factor != 1.0:
                        nc.vector.tensor_scalar(w[:, :, columns], w[:, :, columns], factor, None, ALU.mult) \
                            .then_inc(signal, 1)

            def period(n, g, r, rnn_steps=PHASES):
                for p in range(PHASES):
                    t = g * PHASES + p
                    dve.wait_ge(lstm_z_ready, t + 1)
                    nc.vector.transpose(lstm_z.rearrange("q k c -> q (k c)"), lstm_acc[r][:, 0:MAIN]) \
                        .then_inc(lstm_z_turned, 1)
                    dve.wait_ge(o_z_ready, t + 1)
                    nc.vector.transpose(o_z[:].rearrange("q k c -> q (k c)"), o_acc[r][:, SPARE:WIDE]) \
                        .then_inc(o_z_turned, 1)
                    dve.wait_ge(gates_ready, t + 1)
                    nc.vector.scalar_tensor_tensor(out=terms[:], in0=gates[:, 0:2 * HALVES], scalar=1.0,
                                                   in1=gates[:, 2 * HALVES:4 * HALVES],
                                                   op0=ALU.add, op1=ALU.mult).then_inc(terms_ready, 1)
                    dve.wait_ge(terms_ready, t + 1)
                    def update_c(out):
                        return nc.vector.scalar_tensor_tensor(out=out, in0=terms[:, HALVES:], scalar=0.5,
                                                              in1=terms[:, 0:HALVES], op0=ALU.mult, op1=ALU.add)
                    update_c(new_c).then_inc(c_ready, 1)
                    update_c(gates[:, 3 * HALVES:])
                    dve.wait_ge(tanh_c_ready, t + 1)
                    h = lstm_h[:, (p + 1) % PHASES, :, cols(p + 1)]
                    nc.vector.scalar_tensor_tensor(out=h, in0=tanh_o[:], scalar=1.0,
                                                   in1=tanh_c, op0=ALU.add, op1=ALU.mult).then_inc(lstm_h_ready, 1)
                    if p == 0:
                        dve.wait_ge(slot_free[r], n * 16 + 16)
                    dve.wait_ge(x1_ready, t + 1)
                    dve.wait_ge(lstm_h_ready, t + 2)
                    nc.vector.scalar_tensor_tensor(out=y_down[:, r, :, cols(p)], in0=h, scalar=0.5,
                                                   in1=x1_in[:, r, :, cols(p)],
                                                   op0=ALU.mult, op1=ALU.add).then_inc(y_ready, 1)
                    if p < rnn_steps:
                        rnn_turn(t + LEAD + 1, PHASES * r + p + LEAD)

            chain = [0]

            def link(instruction):
                instruction.then_inc(b_step, 1)
                chain[0] += 1
                dve.wait_ge(b_step, chain[0])

            dve.wait_ge(lstm_b_loaded, 16)
            for gates_of_b in (lstm_b[:, 0:2 * F], lstm_b[:, MAIN:]):
                link(nc.vector.tensor_scalar(gates_of_b, gates_of_b, 0.5, None, ALU.mult))
            for n in range(SPLITS):
                link(nc.vector.tensor_copy(b_split[:, n], lstm_b[:]))
                if n + 1 < SPLITS:
                    link(nc.vector.tensor_tensor(lstm_b[:], lstm_b[:], b_split[:, n], ALU.subtract))
            for s in range(LEAD):
                rnn_turn(s + 1, s)
                if s == 2:
                    dve.wait_ge(lstm_wx_loaded, 16)
                    for k in range(HALVES):
                        scale(lstm_wx[:, k], 0.5, 1.0, lstm_wx_scaled)
            dve.wait_ge(lstm_wh_loaded, 16)
            for k in range(HALVES):
                scale(lstm_wh[:, k], 0.25, 0.5, lstm_wh_scaled)
            with dve.Fori(0, LOOP_GROUPS // RING) as n:
                for r in range(RING):
                    period(n, n * RING + r, r)
            for g in range(LOOP_GROUPS, GROUPS):
                period(g // RING, g, g % RING, rnn_steps=T - LEAD - g * PHASES)

        @block.tensor
        def _(pe):
            def add_product(acc, stationary, columns, start=False):
                m = stationary.shape[-1]
                for j in range(TILES):
                    moving = columns(j)
                    last = nc.tensor.matmul(acc[LANES * j:LANES * j + m, 0:moving.shape[-1]], stationary, moving,
                                            start=start, stop=True, skip_group_check=True,
                                            tile_position=(0, LANES * j))
                return last

            def rnn_columns(w):
                return lambda j: w[:, F * j:F * j + WIDE]

            def main_columns(w):
                return lambda j: w[:, j, 0:MAIN]

            def o_columns(w):
                return lambda j: w[:, j, MAIN - SPARE:MAIN + F]

            def rnn_input(r, stationary):
                for k in range(HALVES):
                    add_product(rnn_acc[r], stationary[:, k], rnn_columns(rnn_wx[:, k]), start=k == 0)

            def lstm_bias(r, start):
                for acc, columns in ((lstm_acc, main_columns), (o_acc, o_columns)):
                    add_product(acc[r], ones[:], columns(lstm_b_parts[:]), start=start)

            def lstm_input(r, k, start=False):
                for acc, columns in ((lstm_acc, main_columns), (o_acc, o_columns)):
                    add_product(acc[r], x1_in[:, r, k], columns(lstm_wx[:, k]), start=start)

            def rnn_step(ready, s):
                r, p = place(s)
                pe.wait_ge(rnn_h_ready, ready)
                for k in range(HALVES):
                    last = add_product(rnn_acc[r], rnn_h[:, s % STEPS, k, 0:BATCH * (p + 1)], rnn_columns(rnn_wh[:, k]))
                last.then_inc(rnn_z_ready, 1)

            def lstm_step(t, r, p):
                m = BATCH * (p + 1)
                pe.wait_ge(lstm_h_ready, t + 1)
                for acc, columns, signal in ((lstm_acc, main_columns, lstm_z_ready), (o_acc, o_columns, o_z_ready)):
                    for k in range(HALVES):
                        last = add_product(acc[r], lstm_h[:, p, k, 0:m], columns(lstm_wh[:, k]))
                    last.then_inc(signal, 1)

            def period(g, r, rnn_steps=PHASES, next_rnn=True, next_lstm=True):
                for p in range(PHASES):
                    t = g * PHASES + p
                    lstm_step(t, r, p)
                    if p < rnn_steps:
                        rnn_step(t + LEAD + 1, PHASES * r + p + LEAD)
                    if next_rnn and p == 0:
                        pe.wait_ge(x_in_ready, g + 2)
                        rnn_input(r, x_in[:, r])
                    if next_lstm and p == 1:
                        lstm_bias((r + 1) % RING, start=True)
                    if next_lstm and p == 2:
                        pe.wait_ge(x1_ready, (g + 2) * PHASES)
                    if next_lstm and p >= 2:
                        lstm_input((r + 1) % RING, p - 2)

            pe.wait_ge(x_loaded, 16)
            pe.wait_ge(rnn_w_zeroed, 2)
            pe.wait_ge(rnn_wx_loaded, 16)
            rnn_input(0, x_down[:, 0])
            rnn_input(1, x_down[:, 1])
            pe.wait_ge(rnn_wh_loaded, 16)
            for s in range(LEAD):
                rnn_step(s + 1, s)
                if s == PHASES:
                    pe.wait_ge(lstm_wx_scaled, 2 * HALVES)
                    pe.wait_ge(x1_ready, PHASES)
                if s >= PHASES:
                    lstm_input(0, s - PHASES, start=s == PHASES)
            pe.wait_ge(ones_ready, 1 + SPLITS)
            pe.wait_ge(lstm_b_ready, 16 * SPLITS)
            lstm_bias(0, start=False)
            pe.wait_ge(lstm_wh_scaled, 3 * HALVES)
            with pe.Fori(0, LOOP_GROUPS // RING) as n:
                for r in range(RING):
                    period(n * RING + r, r)
            for g in range(LOOP_GROUPS, GROUPS):
                period(g, g % RING, rnn_steps=T - LEAD - g * PHASES, next_rnn=g + 2 < GROUPS,
                       next_lstm=g + 1 < GROUPS)


def kernel(x, cond_1024, L0_cond_Wx, L0_cond_Wh, L0_cond_b, L1_cond_Wx, L1_cond_Wh, L1_cond_b):
    import numpy as np
    import concourse.bacc as bacc
    from concourse.bass_utils import run_bass_kernel_spmd

    def down(a):
        return a.reshape(TILES, HALVES, LANES, *a.shape[1:]).swapaxes(1, 2).reshape(TILES * LANES, HALVES, *a.shape[1:])

    def by_tile(w):
        w = w.reshape(*w.shape[:-1], -1, TILES, F)
        w = w[..., [0, 1, 3, 2], :, :] if w.shape[-3] == GATES else w
        w = np.moveaxis(w, -2, -3)
        return w.reshape(*w.shape[:-3], TILES, -1)

    def weights(w):
        return by_tile(down(np.asarray(w)))

    xt = np.asarray(x).reshape(BATCH, GROUPS, PHASES, D).transpose(3, 1, 2, 0).reshape(D, GROUPS, LANES)
    arrays = {
        "x": down(xt).transpose(0, 2, 1, 3),
        "cond": down(np.asarray(cond_1024).T),
        "rnn_wx": down(np.asarray(L0_cond_Wx)), "rnn_wh": down(np.asarray(L0_cond_Wh)),
        "rnn_b": down(np.asarray(L0_cond_b)),
        "lstm_wx": weights(L1_cond_Wx), "lstm_wh": weights(L1_cond_Wh),
        "lstm_b": by_tile(np.asarray(L1_cond_b)),
    }
    arrays = {f"{name}_dram": np.ascontiguousarray(a) for name, a in arrays.items()}
    nc = bacc.Bacc("TRN2", target_bir_lowering=False, num_devices=1)
    args = [nc.dram_tensor(name, a.shape, mybir.dt.from_np(a.dtype), kind="ExternalInput").ap()
            for name, a in arrays.items()]
    out = nc.dram_tensor("y_dram", (TILES * LANES, GROUPS, HALVES, LANES), mybir.dt.float32, kind="ExternalOutput").ap()
    two_layer_program(nc, *args, out)
    got = run_bass_kernel_spmd(nc, [arrays], core_ids=[0]).results[0]["y_dram"]
    got = got.reshape(TILES, LANES, GROUPS, HALVES, PHASES, BATCH).transpose(5, 2, 4, 0, 3, 1)
    return np.ascontiguousarray(got.reshape(BATCH, T, D))
```

```python
import concourse.bass as bass
from concourse import mybir
from contextlib import ExitStack

BATCH, T, D = 8, 256, 256
GATES = 4
TILES, LANES = 4, 32
HALVES = D // (TILES * LANES)
F = HALVES * LANES
PHASES = LANES // BATCH
GROUPS = T // PHASES
HALF0, HALF1 = "ifg", "ifgoo"
BLOCKS = (len(HALF0), len(HALF1))
IFG = 3
GATE_RUNS = ((0, 2, 0.5), (2, 3, 1.0), (3, 5, 0.5), (5, 6, 1.0), (6, 8, 0.5))
G_BLOCKS = (2, 5)
SPARE = 32
WIDE = SPARE + F
SUM_SCALE = 0.25
SPLITS = 3
RING = 2
BODY = 2 * RING
STEPS = RING * PHASES
LEAD = 7
RNN_FIRST = -LEAD % PHASES
LOOP_GROUPS = GROUPS - BODY


def two_layer_program(nc, x, cond, rnn_wx_d, rnn_wh_d, rnn_b_d, lstm_wx_d, lstm_wh_d, lstm_b_d, out):
    fp32, bf16 = mybir.dt.float32, mybir.dt.bfloat16
    ALU = mybir.AluOpType
    TANH = mybir.ActivationFunctionType.Tanh
    COPY = mybir.ActivationFunctionType.Copy

    ctx = ExitStack()
    with ctx:
        def sbuf(name, shape, dtype=fp32):
            return ctx.enter_context(nc.sbuf_tensor(name, shape, dtype))

        def psum(name):
            return ctx.enter_context(nc.psum_tensor(name, [128, 512], fp32))

        def sem(name):
            return ctx.enter_context(nc.semaphore(name))

        rnn_wx = sbuf("rnn_wx", [128, HALVES, SPARE + TILES * F])
        rnn_wh = sbuf("rnn_wh", [128, HALVES, SPARE + TILES * F])
        lstm_wx = sbuf("lstm_wx", [128, HALVES, TILES, GATES * F])
        lstm_wh = sbuf("lstm_wh", [128, HALVES, TILES, GATES * F])
        rnn_b = sbuf("rnn_b", [128, HALVES])
        lstm_b = sbuf("lstm_b", [TILES, GATES * F])
        b_split = sbuf("b_split", [TILES, SPLITS, GATES * F], bf16)
        lstm_b_parts = sbuf("lstm_b_parts", [128, TILES, GATES * F], bf16)
        ones = sbuf("ones", [128, LANES], bf16)
        idle = sbuf("idle", [128, 512], bf16)
        x_down = sbuf("x_down", [128, GROUPS, HALVES, LANES])
        cond_down = sbuf("cond_down", [128, HALVES, BATCH])
        x_in = sbuf("x_in", [128, RING, HALVES, LANES])
        x1_in = sbuf("x1_in", [128, RING, HALVES, LANES])
        rnn_h = sbuf("rnn_h", [128, STEPS, HALVES, LANES])
        lstm_h = sbuf("lstm_h", [128, PHASES, HALVES, LANES])
        gates = [sbuf(f"gates{k}", [128, IFG + 1, BATCH]) for k in range(HALVES)]
        tanh_o = sbuf("tanh_o", [128, HALVES, BATCH])
        terms = [sbuf(f"terms{k}", [128, 2, BATCH]) for k in range(HALVES)]
        y_down = sbuf("y_down", [128, RING, HALVES, LANES])

        rnn_acc = psum("rnn_acc")
        lstm_acc = [[psum(f"lstm_acc{k}_{r}") for r in range(RING)] for k in range(HALVES)]
        banks = [psum(f"bank{k}") for k in range(HALVES)]
        lstm_z = [banks[k][:, 0:IFG * LANES] for k in range(HALVES)]
        new_c = [banks[k][:, 256:256 + BATCH] for k in range(HALVES)]
        tanh_c = [banks[k][:, 320:320 + BATCH] for k in range(HALVES)]
        rnn_z = banks[0][:, 384:384 + F]
        o_bank = psum("o_bank")
        o_z = [o_bank[:, LANES * k:LANES * (k + 1)] for k in range(HALVES)]

        x_loaded = sem("x_loaded")
        x_next_loaded = sem("x_next_loaded")
        x_rest_loaded = sem("x_rest_loaded")
        cond_loaded = sem("cond_loaded")
        rnn_wx_loaded = sem("rnn_wx_loaded")
        rnn_wh_loaded = sem("rnn_wh_loaded")
        lstm_wx_loaded = sem("lstm_wx_loaded")
        lstm_wh_loaded = sem("lstm_wh_loaded")
        rnn_b_loaded = sem("rnn_b_loaded")
        lstm_b_loaded = sem("lstm_b_loaded")
        slot_free = [sem(f"slot_free{r}") for r in range(RING)]
        rnn_w_zeroed = sem("rnn_w_zeroed")
        parts_zeroed = sem("parts_zeroed")
        b_step = sem("b_step")
        lstm_b_ready = sem("lstm_b_ready")
        ones_ready = sem("ones_ready")
        idle_zeroed = sem("idle_zeroed")
        x1_start_zeroed = sem("x1_start_zeroed")
        rnn_h_zeroed = sem("rnn_h_zeroed")
        lstm_h_zeroed = sem("lstm_h_zeroed")
        lstm_wx_scaled = sem("lstm_wx_scaled")
        lstm_wh_scaled = sem("lstm_wh_scaled")
        rnn_z_ready = sem("rnn_z_ready")
        rnn_z_turned = sem("rnn_z_turned")
        rnn_h_ready = [sem(f"rnn_h_ready{k}") for k in range(HALVES)]
        x1_ready = sem("x1_ready")

        def sems(name):
            return [sem(f"{name}{k}") for k in range(HALVES)]

        lstm_z_ready = sems("lstm_z_ready")
        lstm_z_turned = sems("lstm_z_turned")
        gates_ready = sems("gates_ready")
        terms_ready = sems("terms_ready")
        c_ready = sems("c_ready")
        tanh_c_ready = sems("tanh_c_ready")
        lstm_h_ready = sems("lstm_h_ready")
        o_z_turned = sems("o_z_turned")
        o_ready = sem("o_ready")
        y_ready = sem("y_ready")
        x_in_ready = sem("x_in_ready")

        FIRST_X, NEXT_X = 2, 3 + RING

        def cols(p):
            return slice(BATCH * (p % PHASES), BATCH * (p % PHASES + 1))

        def place(s):
            return s // PHASES % RING, s % PHASES

        block = ctx.enter_context(nc.Block())

        @block.sync
        def _(sp):
            sp.dma_start(x_down[:, 0:FIRST_X], x[:, 0:FIRST_X]).then_inc(x_loaded, 16)
            sp.dma_start(rnn_wx[:, :, SPARE:], rnn_wx_d).then_inc(rnn_wx_loaded, 16)
            sp.dma_start(rnn_wh[:, :, SPARE:], rnn_wh_d).then_inc(rnn_wh_loaded, 16)
            sp.dma_start(lstm_wx[:], lstm_wx_d).then_inc(lstm_wx_loaded, 16)
            sp.dma_start(x_down[:, FIRST_X:NEXT_X], x[:, FIRST_X:NEXT_X]).then_inc(x_next_loaded, 16)
            sp.dma_start(lstm_wh[:], lstm_wh_d).then_inc(lstm_wh_loaded, 16)
            sp.wait_ge(parts_zeroed, 1)
            sp.wait_ge(b_step, len(GATE_RUNS) + 2 * SPLITS - 1)
            for n in range(SPLITS):
                sp.dma_start(lstm_b_parts[LANES * n:LANES * n + 1], b_split[:, n]).then_inc(lstm_b_ready, 16)
            sp.dma_start(x_down[:, NEXT_X:GROUPS], x[:, NEXT_X:GROUPS]).then_inc(x_rest_loaded, 16)

            def store(g, r):
                sp.wait_ge(y_ready, g * PHASES + PHASES + 1)
                sp.dma_start(out[:, bass.ds(g, 1)], y_down[:, r:r + 1]).then_inc(slot_free[r], 16)

            with sp.Fori(0, GROUPS // RING) as n:
                for r in range(RING):
                    store(n * RING + r, r)
            for r in range(RING):
                sp.wait_ge(slot_free[r], 16 + 16 * GROUPS // RING)

        @block.gpsimd
        def _(pool):
            nc.gpsimd.memset(lstm_b_parts[:], 0.0).then_inc(parts_zeroed, 1)

            def add_x1(x_group, s):
                r, p = place(s)
                nc.gpsimd.tensor_tensor(x1_in[:, r, :, cols(p)], x_group[:, :, cols(p)],
                                        rnn_h[:, (s + 1) % STEPS, :, cols(p + 1)], ALU.add).then_inc(x1_ready, 1)

            def copy_x(g, r):
                nc.gpsimd.tensor_copy(x_in[:, r], x_down[:, bass.ds(g, 1)].rearrange("q o k c -> q (o k) c")) \
                    .then_inc(x_in_ready, 1)

            def period(g, r, steps=PHASES, next_x=True):
                for p in range(steps):
                    if p == RNN_FIRST:
                        pool.wait_ge(x_in_ready, g + 2)
                        pool.wait_ge(x1_ready, (g + 2) * PHASES)
                    pool.wait_ge(y_ready, g * PHASES + p + 1)
                    pool.wait_ge(rnn_h_ready[1], g * PHASES + p + LEAD + 2)
                    add_x1(x_in[:, place(PHASES * r + p + LEAD)[0]], PHASES * r + p + LEAD)
                    if next_x and p == RNN_FIRST:
                        copy_x(g + 3, (r + 1) % RING)

            pool.wait_ge(x_loaded, 16)
            for s in range(LEAD):
                pool.wait_ge(rnn_h_ready[1], s + 2)
                add_x1(x_down[:, s // PHASES], s)
            copy_x(1, 1)
            pool.wait_ge(x_next_loaded, 16)
            copy_x(2, 0)
            pool.wait_ge(x_in_ready, 2)
            for g in range(RING):
                period(g, g)
            pool.wait_ge(x_rest_loaded, 16)
            with pool.Fori(1, LOOP_GROUPS // RING) as n:
                for r in range(RING):
                    period(n * RING + r, r)
            for g in range(LOOP_GROUPS, GROUPS - 1):
                period(g, g % RING, steps=min(PHASES, T - LEAD - g * PHASES), next_x=g + 3 < GROUPS)

        @block.scalar
        def _(act):
            act.dma_start(cond_down[:], cond).then_inc(cond_loaded, 16)
            for signal in (*lstm_z_turned, *o_z_turned):
                act.sem_inc(signal, 1)
            act.dma_start(rnn_b[:], rnn_b_d).then_inc(rnn_b_loaded, 16)
            act.dma_start(lstm_b[:], lstm_b_d).then_inc(lstm_b_loaded, 16)
            act.wait_ge(cond_loaded, 16)
            act.wait_ge(rnn_h_zeroed, 1)
            for k in range(HALVES):
                nc.scalar.activation(rnn_h[:, 0, k, cols(0)], cond_down[:, k], COPY).then_inc(rnn_h_ready[k], 1)

            def rnn_tanh(done, s):
                p = s % PHASES
                act.wait_ge(rnn_z_turned, done)
                z = rnn_z.rearrange("q (k c) -> q k c", c=LANES)
                for k in range(HALVES):
                    nc.scalar.activation(rnn_h[:, (s + 1) % STEPS, k, cols(p + 1)], z[:, k, cols(p)], TANH,
                                         bias=rnn_b[:, k:k + 1]).then_inc(rnn_h_ready[k], 1)

            def period(g, r, rnn_steps=PHASES):
                for p in range(PHASES):
                    t = g * PHASES + p
                    for k in range(HALVES):
                        act.wait_ge(lstm_z_turned[k], t + 2)
                        z = lstm_z[k].rearrange("q (n c) -> q n c", c=LANES)[:, :, cols(p)]
                        nc.scalar.activation(gates[k][:, 0:IFG], z, TANH, scale=SUM_SCALE).then_inc(gates_ready[k], 1)
                    for k in range(HALVES):
                        act.wait_ge(o_z_turned[k], t + 2)
                        o = nc.scalar.activation(tanh_o[:, k], o_z[k][:, cols(p)], TANH, scale=SUM_SCALE)
                        if k == 0:
                            o.then_inc(o_ready, 1)
                        act.wait_ge(c_ready[k], t + 2)
                        nc.scalar.activation(tanh_c[k], new_c[k], TANH, scale=0.5).then_inc(tanh_c_ready[k], 1)
                    if p < rnn_steps:
                        rnn_tanh(t + LEAD + 1, PHASES * r + p + LEAD)

            act.wait_ge(rnn_b_loaded, 16)
            for s in range(LEAD):
                rnn_tanh(s + 1, s)
            with act.Fori(0, LOOP_GROUPS // BODY) as n:
                for i in range(BODY):
                    period(n * BODY + i, i % RING)
            for g in range(LOOP_GROUPS, GROUPS):
                period(g, g % RING, rnn_steps=T - LEAD - g * PHASES)

        @block.vector
        def _(dve):
            nc.vector.memset(idle[:], 0.0).then_inc(idle_zeroed, 1)
            for signal in (*lstm_z_ready, *gates_ready, *terms_ready, *tanh_c_ready, o_ready):
                dve.sem_inc(signal, 1)
            nc.vector.memset(rnn_h[:], 0.0).then_inc(rnn_h_zeroed, 1)
            nc.vector.memset(ones[:], 0.0).then_inc(ones_ready, 1)
            dve.wait_ge(ones_ready, 1)
            for n in range(SPLITS):
                nc.vector.memset(ones[LANES * n:LANES * n + 1], 1.0).then_inc(ones_ready, 1)
            nc.vector.memset(rnn_wx[:, :, 0:SPARE], 0.0).then_inc(rnn_w_zeroed, 1)
            nc.vector.memset(rnn_wh[:, :, 0:SPARE], 0.0).then_inc(rnn_w_zeroed, 1)
            nc.vector.memset(lstm_h[:], 0.0).then_inc(lstm_h_zeroed, 1)
            nc.vector.memset(gates[0][:, IFG:], 0.0).then_inc(c_ready[0], 1)
            nc.vector.memset(terms[1][:], 0.0).then_inc(c_ready[1], 1)
            for r in range(RING):
                nc.vector.memset(y_down[:, r], 0.0).then_inc(slot_free[r], 16)
            nc.vector.memset(x1_in[:, RING - 1, :, cols(PHASES - 1)], 0.0).then_inc(x1_start_zeroed, 1)
            dve.wait_ge(x1_start_zeroed, 1)
            dve.wait_ge(cond_loaded, 16)
            dve.wait_ge(lstm_h_zeroed, 1)
            for k in range(HALVES):
                nc.vector.tensor_scalar(lstm_h[:, 0, k, cols(0)], cond_down[:, k], 2.0, None, ALU.mult) \
                    .then_inc(lstm_h_ready[k], 1)

            def rnn_turn(done, s):
                dve.wait_ge(rnn_z_ready, done)
                nc.vector.transpose(rnn_z, rnn_acc[:, SPARE:WIDE]).then_inc(rnn_z_turned, 1)

            def scale(w, first, end, factor, signal):
                run = w[..., LANES * first:LANES * end]
                nc.vector.tensor_scalar(run, run, factor, None, ALU.mult).then_inc(signal, 1)

            def scale_all(w, signal):
                for first, end, factor in GATE_RUNS:
                    scale(w, first, end, factor / SUM_SCALE, signal)

            def turn(k, t, r):
                dve.wait_ge(lstm_z_ready[k], t + 2)
                nc.vector.transpose(lstm_z[k], lstm_acc[k][r][:, 0:IFG * LANES]).then_inc(lstm_z_turned[k], 1)

            def turn_o(k, r):
                first = (IFG + k) * LANES
                nc.vector.transpose(o_z[k], lstm_acc[1][r][:, first:first + LANES]).then_inc(o_z_turned[k], 1)

            def make_terms(k, t):
                dve.wait_ge(gates_ready[k], t + 2)
                nc.vector.scalar_tensor_tensor(out=terms[k][:], in0=gates[k][:, 0:2], scalar=1.0,
                                               in1=gates[k][:, 2:4],
                                               op0=ALU.add, op1=ALU.mult).then_inc(terms_ready[k], 1)

            def update(k, out):
                return nc.vector.scalar_tensor_tensor(out=out, in0=terms[k][:, 1], scalar=0.5,
                                                      in1=terms[k][:, 0], op0=ALU.mult, op1=ALU.add)

            def make_c(k, t):
                dve.wait_ge(terms_ready[k], t + 2)
                update(k, new_c[k]).then_inc(c_ready[k], 1)

            def keep_c(k):
                update(k, gates[k][:, IFG])

            def make_h(k, t, p):
                dve.wait_ge(tanh_c_ready[k], t + 2)
                nc.vector.scalar_tensor_tensor(out=lstm_h[:, (p + 1) % PHASES, k, cols(p + 1)],
                                               in0=tanh_o[:, k], scalar=1.0, in1=tanh_c[k],
                                               op0=ALU.add, op1=ALU.mult).then_inc(lstm_h_ready[k], 1)

            def make_y(s):
                r, p = place(s % STEPS)
                nc.vector.scalar_tensor_tensor(out=y_down[:, r, :, cols(p)],
                                               in0=lstm_h[:, (p + 1) % PHASES, :, cols(p + 1)], scalar=0.5,
                                               in1=x1_in[:, r, :, cols(p)],
                                               op0=ALU.mult, op1=ALU.add).then_inc(y_ready, 1)

            def period(use, g, r, rnn_steps=PHASES):
                for p in range(PHASES):
                    t = g * PHASES + p
                    if p <= rnn_steps:
                        dve.wait_ge(rnn_h_ready[1], t + LEAD + 1)
                    keep_c(1)
                    turn(0, t, r)
                    turn(1, t, r)
                    make_terms(0, t)
                    turn_o(0, r)
                    make_c(0, t)
                    keep_c(0)
                    make_terms(1, t)
                    dve.wait_ge(o_ready, t + 2)
                    turn_o(1, r)
                    make_h(0, t, p)
                    make_c(1, t)
                    if p < rnn_steps:
                        rnn_turn(t + LEAD + 1, PHASES * r + p + LEAD)
                    if p == 1:
                        dve.wait_ge(slot_free[r], use * 16 + 16)
                    make_y(PHASES * r + p - 1)
                    make_h(1, t, p)

            chain = [0]

            def link(instruction):
                instruction.then_inc(b_step, 1)
                chain[0] += 1
                dve.wait_ge(b_step, chain[0])

            dve.wait_ge(lstm_b_loaded, 16)
            scale_all(lstm_b[:], b_step)
            chain[0] = len(GATE_RUNS)
            dve.wait_ge(b_step, chain[0])
            for n in range(SPLITS):
                link(nc.vector.tensor_copy(b_split[:, n], lstm_b[:]))
                if n + 1 < SPLITS:
                    link(nc.vector.tensor_tensor(lstm_b[:], lstm_b[:], b_split[:, n], ALU.subtract))
                if n == 0:
                    rnn_turn(1, 0)
            for s in range(1, LEAD):
                rnn_turn(s + 1, s)
                if s in (2, 3):
                    dve.wait_ge(lstm_wx_loaded, 16)
                    scale_all(lstm_wx[:, s - 2], lstm_wx_scaled)
                if s == 4:
                    dve.wait_ge(lstm_wh_loaded, 16)
                    for n in G_BLOCKS:
                        for k in range(HALVES):
                            scale(lstm_wh[:, k], n, n + 1, 2.0, lstm_wh_scaled)
            with dve.Fori(0, LOOP_GROUPS // BODY) as n:
                for i in range(BODY):
                    period(n * (BODY // RING) + i // RING, n * BODY + i, i % RING)
            for g in range(LOOP_GROUPS, GROUPS):
                period(g // RING, g, g % RING, rnn_steps=T - LEAD - g * PHASES)
            dve.wait_ge(lstm_h_ready[1], T + 1)
            make_y(T - 1)

        @block.tensor
        def _(pe):
            def add_product(acc, stationary, columns, start=False):
                m = stationary.shape[-1]
                for j in range(TILES):
                    moving = columns(j)
                    last = nc.tensor.matmul(acc[LANES * j:LANES * j + m, 0:moving.shape[-1]], stationary, moving,
                                            start=start, stop=True, skip_group_check=True,
                                            tile_position=(0, LANES * j))
                return last

            def keep_warm(acc, times):
                for _ in range(times):
                    nc.tensor.matmul(acc[0:LANES, :], idle[:, 0:LANES], idle[:],
                                     start=True, stop=True, skip_group_check=True, tile_position=(0, 0))

            def rnn_columns(w):
                return lambda j: w[:, F * j:F * j + WIDE]

            def half_columns(w, k):
                first = sum(BLOCKS[:k]) * LANES
                return lambda j: w[:, j, first:first + BLOCKS[k] * LANES]

            def rnn_input(stationary):
                for k in range(HALVES):
                    add_product(rnn_acc, stationary[:, k], rnn_columns(rnn_wx[:, k]), start=k == 0)

            def lstm_bias(r, start):
                for half in range(HALVES):
                    add_product(lstm_acc[half][r], ones[:], half_columns(lstm_b_parts[:], half), start=start)

            def lstm_input(r, k, start=False):
                for half in range(HALVES):
                    add_product(lstm_acc[half][r], x1_in[:, r, k], half_columns(lstm_wx[:, k], half), start=start)

            def rnn_step(ready, s, group_x=None):
                p = s % PHASES
                if group_x is not None:
                    pe.wait_ge(rnn_z_turned, ready - 1)
                    rnn_input(group_x)
                for k in range(HALVES):
                    pe.wait_ge(rnn_h_ready[k], ready)
                    last = add_product(rnn_acc, rnn_h[:, s % STEPS, k, 0:BATCH * (p + 1)], rnn_columns(rnn_wh[:, k]))
                last.then_inc(rnn_z_ready, 1)

            def lstm_step(t, r, p):
                m = BATCH * (p + 1)
                for k in range(HALVES):
                    pe.wait_ge(lstm_h_ready[k], t + 1)
                    for half in range(HALVES):
                        last = add_product(lstm_acc[half][r], lstm_h[:, p, k, 0:m], half_columns(lstm_wh[:, k], half))
                        if k == HALVES - 1:
                            last.then_inc(lstm_z_ready[half], 1)

            def period(g, r, rnn_steps=PHASES, next_lstm=True):
                for p in range(PHASES):
                    t = g * PHASES + p
                    lstm_step(t, r, p)
                    if p < rnn_steps:
                        new_group = p == RNN_FIRST
                        if new_group:
                            pe.wait_ge(x_in_ready, g + 2)
                        rnn_step(t + LEAD + 1, PHASES * r + p + LEAD, x_in[:, r] if new_group else None)
                    elif t < T - 1:
                        keep_warm(rnn_acc, 2 if next_lstm else 4)
                    if next_lstm and p == 0:
                        lstm_bias((r + 1) % RING, start=True)
                    if next_lstm and p == 2:
                        pe.wait_ge(x1_ready, (g + 2) * PHASES)
                    if next_lstm and p >= 2:
                        lstm_input((r + 1) % RING, p - 2)

            pe.wait_ge(idle_zeroed, 1)
            spare_bank = lstm_acc[1][1]
            keep_warm(spare_bank, 8)
            pe.wait_ge(x_loaded, 16)
            pe.wait_ge(rnn_w_zeroed, 2)
            pe.wait_ge(rnn_wx_loaded, 16)
            rnn_input(x_down[:, 0])
            pe.wait_ge(rnn_wh_loaded, 16)
            for s in range(LEAD):
                if s == LEAD - 2:
                    pe.wait_ge(lstm_wx_scaled, len(GATE_RUNS) * HALVES)
                    pe.wait_ge(x1_ready, PHASES)
                if s >= LEAD - 2:
                    k = s - (LEAD - 2)
                    lstm_input(0, k, start=k == 0)
                if s == LEAD - 1:
                    pe.wait_ge(ones_ready, 1 + SPLITS)
                    pe.wait_ge(lstm_b_ready, 16 * SPLITS)
                    lstm_bias(0, start=False)
                rnn_step(s + 1, s, x_down[:, 1] if s == PHASES else None)
                if s < LEAD - 3:
                    keep_warm(spare_bank, 3)
            pe.wait_ge(lstm_wh_scaled, len(G_BLOCKS) * HALVES)
            with pe.Fori(0, LOOP_GROUPS // BODY) as n:
                for i in range(BODY):
                    period(n * BODY + i, i % RING)
            for g in range(LOOP_GROUPS, GROUPS):
                period(g, g % RING, rnn_steps=T - LEAD - g * PHASES, next_lstm=g + 1 < GROUPS)


def kernel(x, cond_1024, L0_cond_Wx, L0_cond_Wh, L0_cond_b, L1_cond_Wx, L1_cond_Wh, L1_cond_b):
    import numpy as np
    import concourse.bacc as bacc
    from concourse.bass_utils import run_bass_kernel_spmd

    def down(a):
        return a.reshape(TILES, HALVES, LANES, *a.shape[1:]).swapaxes(1, 2).reshape(TILES * LANES, HALVES, *a.shape[1:])

    def by_tile(w):
        w = w.reshape(*w.shape[:-1], GATES, TILES, HALVES, LANES)
        order = [("ifog".index(gate), 0) for gate in HALF0]
        order += [("ifog".index(gate), n - IFG if gate == "o" else 1) for n, gate in enumerate(HALF1)]
        return np.stack([w[..., gate, :, k, :] for gate, k in order], axis=-2).reshape(*w.shape[:-4], TILES, -1)

    def weights(w):
        return by_tile(down(np.asarray(w)))

    xt = np.asarray(x).reshape(BATCH, GROUPS, PHASES, D).transpose(3, 1, 2, 0).reshape(D, GROUPS, LANES)
    arrays = {
        "x": down(xt).transpose(0, 2, 1, 3),
        "cond": down(np.asarray(cond_1024).T),
        "rnn_wx": down(np.asarray(L0_cond_Wx)), "rnn_wh": down(np.asarray(L0_cond_Wh)),
        "rnn_b": down(np.asarray(L0_cond_b)),
        "lstm_wx": weights(L1_cond_Wx), "lstm_wh": weights(L1_cond_Wh),
        "lstm_b": by_tile(np.asarray(L1_cond_b)),
    }
    arrays = {f"{name}_dram": np.ascontiguousarray(a) for name, a in arrays.items()}
    nc = bacc.Bacc("TRN2", target_bir_lowering=False, num_devices=1)
    args = [nc.dram_tensor(name, a.shape, mybir.dt.from_np(a.dtype), kind="ExternalInput").ap()
            for name, a in arrays.items()]
    out = nc.dram_tensor("y_dram", (TILES * LANES, GROUPS, HALVES, LANES), mybir.dt.float32, kind="ExternalOutput").ap()
    two_layer_program(nc, *args, out)
    got = run_bass_kernel_spmd(nc, [arrays], core_ids=[0]).results[0]["y_dram"]
    got = got.reshape(TILES, LANES, GROUPS, HALVES, PHASES, BATCH).transpose(5, 2, 4, 0, 3, 1)
    return np.ascontiguousarray(got.reshape(BATCH, T, D))
```
